# Optimizing a Trainium2 kernel written in Bass

```python
import numpy as np
import jax
import jax.numpy as jnp

def _softmax(x, axis=-1):
    return jax.nn.softmax(x, axis=axis)

def _gelu(x):
    return jax.nn.gelu(x, approximate=True)

def _silu(x):
    return jax.nn.silu(x)

def _sigmoid(x):
    return jax.nn.sigmoid(x)

def _layernorm(x, axis=-1, eps=1e-05):
    m = jnp.mean(x, axis=axis, keepdims=True)
    v = jnp.var(x, axis=axis, keepdims=True)
    return (x - m) / jnp.sqrt(v + eps)

def _scatter_add(tgt, idx, src, axis=0):
    return tgt.at[idx].add(src)

def _segment_sum(src, seg, n):
    return jax.ops.segment_sum(src, seg, n)
kernel_name = 'mk_dlrm_tower_d1_rec_r8_d1968b'

def setup_inputs(seed: int=0):
    np.random.seed(seed)
    _w = jnp.asarray

    def _rec_inputs():
        import jax
        import jax.numpy as jnp
        _tk = jax.random.key(seed)
        ids = jnp.stack([jax.random.randint(jax.random.fold_in(_tk, 200 + f), (512,), 0, v, jnp.int32) for f, v in enumerate([1250, 12500, 1000, 1250, 1000, 1250, 1000, 125000, 1000, 1000, 1250, 12500, 12500, 1000, 1250, 12500, 1250, 1000, 12500, 1000, 12500, 12500, 1000, 12500, 1000, 1000])], axis=1)
        tbl_0 = 0.05 * jax.random.normal(jax.random.fold_in(_tk, 500 + 0), (1250, 128), jnp.float32)
        tbl_1 = 0.05 * jax.random.normal(jax.random.fold_in(_tk, 500 + 1), (12500, 128), jnp.float32)
        tbl_2 = 0.05 * jax.random.normal(jax.random.fold_in(_tk, 500 + 2), (1000, 128), jnp.float32)
        tbl_3 = 0.05 * jax.random.normal(jax.random.fold_in(_tk, 500 + 3), (1250, 128), jnp.float32)
        tbl_4 = 0.05 * jax.random.normal(jax.random.fold_in(_tk, 500 + 4), (1000, 128), jnp.float32)
        tbl_5 = 0.05 * jax.random.normal(jax.random.fold_in(_tk, 500 + 5), (1250, 128), jnp.float32)
        tbl_6 = 0.05 * jax.random.normal(jax.random.fold_in(_tk, 500 + 6), (1000, 128), jnp.float32)
        tbl_7 = 0.05 * jax.random.normal(jax.random.fold_in(_tk, 500 + 7), (125000, 128), jnp.float32)
        tbl_8 = 0.05 * jax.random.normal(jax.random.fold_in(_tk, 500 + 8), (1000, 128), jnp.float32)
        tbl_9 = 0.05 * jax.random.normal(jax.random.fold_in(_tk, 500 + 9), (1000, 128), jnp.float32)
        tbl_10 = 0.05 * jax.random.normal(jax.random.fold_in(_tk, 500 + 10), (1250, 128), jnp.float32)
        tbl_11 = 0.05 * jax.random.normal(jax.random.fold_in(_tk, 500 + 11), (12500, 128), jnp.float32)
        tbl_12 = 0.05 * jax.random.normal(jax.random.fold_in(_tk, 500 + 12), (12500, 128), jnp.float32)
        tbl_13 = 0.05 * jax.random.normal(jax.random.fold_in(_tk, 500 + 13), (1000, 128), jnp.float32)
        tbl_14 = 0.05 * jax.random.normal(jax.random.fold_in(_tk, 500 + 14), (1250, 128), jnp.float32)
        tbl_15 = 0.05 * jax.random.normal(jax.random.fold_in(_tk, 500 + 15), (12500, 128), jnp.float32)
        tbl_16 = 0.05 * jax.random.normal(jax.random.fold_in(_tk, 500 + 16), (1250, 128), jnp.float32)
        tbl_17 = 0.05 * jax.random.normal(jax.random.fold_in(_tk, 500 + 17), (1000, 128), jnp.float32)
        tbl_18 = 0.05 * jax.random.normal(jax.random.fold_in(_tk, 500 + 18), (12500, 128), jnp.float32)
        tbl_19 = 0.05 * jax.random.normal(jax.random.fold_in(_tk, 500 + 19), (1000, 128), jnp.float32)
        tbl_20 = 0.05 * jax.random.normal(jax.random.fold_in(_tk, 500 + 20), (12500, 128), jnp.float32)
        tbl_21 = 0.05 * jax.random.normal(jax.random.fold_in(_tk, 500 + 21), (12500, 128), jnp.float32)
        tbl_22 = 0.05 * jax.random.normal(jax.random.fold_in(_tk, 500 + 22), (1000, 128), jnp.float32)
        tbl_23 = 0.05 * jax.random.normal(jax.random.fold_in(_tk, 500 + 23), (12500, 128), jnp.float32)
        tbl_24 = 0.05 * jax.random.normal(jax.random.fold_in(_tk, 500 + 24), (1000, 128), jnp.float32)
        tbl_25 = 0.05 * jax.random.normal(jax.random.fold_in(_tk, 500 + 25), (1000, 128), jnp.float32)
        _rk = jax.random.fold_in(_tk, 7)
        r_bottom_output = -0.000520686 + 1.00062 * jax.random.normal(jax.random.fold_in(_rk, 101), (512, 128), jnp.float32)
        W_top1 = 0.0456912 * jax.random.normal(jax.random.fold_in(_tk, 801), (479, 512), jnp.float32)
        W_top2 = 0.0441942 * jax.random.normal(jax.random.fold_in(_tk, 802), (512, 256), jnp.float32)
        W_top3 = 0.0625 * jax.random.normal(jax.random.fold_in(_tk, 803), (256, 1), jnp.float32)
        b_top1 = jnp.zeros((512,), jnp.float32)
        b_top2 = jnp.zeros((256,), jnp.float32)
        return (r_bottom_output, ids, tbl_0, tbl_1, tbl_2, tbl_3, tbl_4, tbl_5, tbl_6, tbl_7, tbl_8, tbl_9, tbl_10, tbl_11, tbl_12, tbl_13, tbl_14, tbl_15, tbl_16, tbl_17, tbl_18, tbl_19, tbl_20, tbl_21, tbl_22, tbl_23, tbl_24, tbl_25, W_top1, b_top1, W_top2, b_top2, W_top3)
    r_bottom_output, ids, tbl_0, tbl_1, tbl_2, tbl_3, tbl_4, tbl_5, tbl_6, tbl_7, tbl_8, tbl_9, tbl_10, tbl_11, tbl_12, tbl_13, tbl_14, tbl_15, tbl_16, tbl_17, tbl_18, tbl_19, tbl_20, tbl_21, tbl_22, tbl_23, tbl_24, tbl_25, W_top1, b_top1, W_top2, b_top2, W_top3 = _rec_inputs()

    def _L0_rec_setup():
        import jax, jax.numpy as jnp
        import numpy as np
        NUM_FEATURES = 27
        _TRIU_I, _TRIU_J = np.triu_indices(NUM_FEATURES, k=1)
        key = jax.random.key(seed)
        k1, k2 = jax.random.split(key)
        bottom_output = jax.random.normal(k1, (2048, 128), dtype=jnp.float32)
        embeddings = jax.random.normal(k2, (2048, 26, 128), dtype=jnp.float32)
        return {'bottom_output': bottom_output, 'embeddings': embeddings}
    _L0_rec_all = _L0_rec_setup()
    _L0_rec_in = {k: v for k, v in _L0_rec_all.items() if k in ()}
    del _L0_rec_all
    return {'r_bottom_output': r_bottom_output, 'ids': ids, 'tbl_0': tbl_0, 'tbl_1': tbl_1, 'tbl_2': tbl_2, 'tbl_3': tbl_3, 'tbl_4': tbl_4, 'tbl_5': tbl_5, 'tbl_6': tbl_6, 'tbl_7': tbl_7, 'tbl_8': tbl_8, 'tbl_9': tbl_9, 'tbl_10': tbl_10, 'tbl_11': tbl_11, 'tbl_12': tbl_12, 'tbl_13': tbl_13, 'tbl_14': tbl_14, 'tbl_15': tbl_15, 'tbl_16': tbl_16, 'tbl_17': tbl_17, 'tbl_18': tbl_18, 'tbl_19': tbl_19, 'tbl_20': tbl_20, 'tbl_21': tbl_21, 'tbl_22': tbl_22, 'tbl_23': tbl_23, 'tbl_24': tbl_24, 'tbl_25': tbl_25, 'W_top1': W_top1, 'b_top1': b_top1, 'W_top2': W_top2, 'b_top2': b_top2, 'W_top3': W_top3}

def reference(r_bottom_output, ids, tbl_0, tbl_1, tbl_2, tbl_3, tbl_4, tbl_5, tbl_6, tbl_7, tbl_8, tbl_9, tbl_10, tbl_11, tbl_12, tbl_13, tbl_14, tbl_15, tbl_16, tbl_17, tbl_18, tbl_19, tbl_20, tbl_21, tbl_22, tbl_23, tbl_24, tbl_25, W_top1, b_top1, W_top2, b_top2, W_top3):
    import jax
    import jax.numpy as jnp

    def _L0_rec_ref(bottom_output, embeddings):
        import jax, jax.numpy as jnp
        import numpy as np
        NUM_FEATURES = 27
        _TRIU_I, _TRIU_J = np.triu_indices(NUM_FEATURES, k=1)
        all_emb = jnp.concatenate([bottom_output[:, None, :], embeddings], axis=1)
        gram = jnp.einsum('bfd,bgd->bfg', all_emb, all_emb)
        return gram[:, _TRIU_I, _TRIU_J]
    e = jnp.stack([tbl_0[ids[:, 0]], tbl_1[ids[:, 1]], tbl_2[ids[:, 2]], tbl_3[ids[:, 3]], tbl_4[ids[:, 4]], tbl_5[ids[:, 5]], tbl_6[ids[:, 6]], tbl_7[ids[:, 7]], tbl_8[ids[:, 8]], tbl_9[ids[:, 9]], tbl_10[ids[:, 10]], tbl_11[ids[:, 11]], tbl_12[ids[:, 12]], tbl_13[ids[:, 13]], tbl_14[ids[:, 14]], tbl_15[ids[:, 15]], tbl_16[ids[:, 16]], tbl_17[ids[:, 17]], tbl_18[ids[:, 18]], tbl_19[ids[:, 19]], tbl_20[ids[:, 20]], tbl_21[ids[:, 21]], tbl_22[ids[:, 22]], tbl_23[ids[:, 23]], tbl_24[ids[:, 24]], tbl_25[ids[:, 25]]], axis=1)
    z = _L0_rec_ref(r_bottom_output, e)
    z = z.reshape(z.shape[0], -1)
    h = jnp.concatenate([z, r_bottom_output], axis=1)
    h = jnp.maximum(h @ W_top1 + b_top1, 0.0)
    h = jnp.maximum(h @ W_top2 + b_top2, 0.0)
    y = h @ W_top3
    return y

_drawn_inputs = setup_inputs


def setup_inputs(seed=0):
    import zlib

    import numpy as np

    out = dict(_drawn_inputs(seed))
    spreads = {'b_top1': (0.0, 0.1), 'b_top2': (0.0, 0.1)}
    factors = {}
    for name, (base, spread) in spreads.items():
        noise = np.random.default_rng([zlib.crc32(name.encode()), seed]).standard_normal(out[name].shape)
        drawn = base * np.exp(spread * noise) if base else spread * noise
        out[name] = jnp.asarray(drawn.astype(out[name].dtype))
    for name, factor in factors.items():
        out[name] = (out[name] * factor).astype(out[name].dtype)
    return out
```

```python
from contextlib import ExitStack

import concourse.bass as bass
from concourse import mybir

ALU = mybir.AluOpType
ACT = mybir.ActivationFunctionType
F32 = mybir.dt.float32
I32 = mybir.dt.int32

P = 128
Q = 32
TABLES = 26
F = TABLES + 1
HALF = F // 2
PAIRS = HALF * F
CH = 3
KP = PAIRS // CH
BLK = P // Q
GRP = 4
BANK = 512


def pair_order():
    rows = []
    for step in range(1, HALF + 1):
        for f in range(F):
            lo, hi = sorted((f, (f + step) % F))
            rows.append(lo * F - lo * (lo + 1) // 2 + hi - lo - 1)
    return rows


def dlrm(nc, bottom, ids, tables, w_pairs, w_bottom, b1, w2, b2, w3, out):
    B, D = bottom.shape
    N1 = w_pairs.shape[1]
    N2 = w2.shape[1]
    T = B // P
    K2 = N1 // P
    GROUPS = [range(f, min(f + GRP, F)) for f in range(0, F, GRP)]
    NG = len(GROUPS)
    QB = Q // 2

    with ExitStack() as ctx:
        def sb(name, shape, dt=F32):
            return ctx.enter_context(nc.sbuf_tensor(name, shape, dt))

        def ps(name, shape):
            return ctx.enter_context(nc.psum_tensor(name, shape, F32))

        def sem(name):
            return ctx.enter_context(nc.semaphore(name))

        idx = sb("idx", [P, T, TABLES], I32)
        rows = sb("rows", [P, T, F, D])
        ident = sb("ident", [P, P])
        emb = sb("emb", [P, T, P * F + 8])
        gram = sb("gram", [P, 2, F + HALF, Q])
        pairs = sb("pairs", [P, 2, PAIRS])
        zt = sb("zt", [P, 2, CH, P])
        h1 = sb("h1", [P, 2, N1])
        h1t = sb("h1t", [P, 2, K2, P])
        h2 = sb("h2", [P, 2, N2])
        prod = sb("prod", [P, 2, N2])
        y = sb("y", [P, T])
        w1s = sb("w1s", [P, CH + 1, N1])
        w2s = sb("w2s", [P, K2, N2])
        w3s = sb("w3s", [P, N2])
        b2s = sb("b2s", [1, N2])
        ones = sb("ones", [1, P])

        psT = [ps(f"psT{i}", [P, BANK]) for i in range(2)]
        psG = ps("psG", [P, 2, BANK])
        psA = ps("psA", [P, BANK])
        psB = ps("psB", [P, BANK])

        ids_in = sem("ids_in")
        bottom_in = sem("bottom_in")
        w1_in = sem("w1_in")
        w2_in = sem("w2_in")
        w3_in = sem("w3_in")
        rows_in = [[sem(f"rows_in_{t}_{g}") for g in range(NG)] for t in range(T)]
        ident_zero = sem("ident_zero")
        ident_ok = sem("ident_ok")
        pads_ok = sem("pads_ok")
        turned = sem("turned")
        emb_ok = sem("emb_ok")
        gram_ok = sem("gram_ok")
        gram_out = sem("gram_out")
        wrap_ok = sem("wrap_ok")
        pairs_ok = sem("pairs_ok")
        zt_ps = sem("zt_ps")
        zt_ok = sem("zt_ok")
        h1_ps = sem("h1_ps")
        h1_ok = sem("h1_ok")
        h1t_ps = sem("h1t_ps")
        h1t_ok = sem("h1t_ok")
        h2_ps = sem("h2_ps")
        h2_ok = sem("h2_ok")
        y_ok = sem("y_ok")
        y_out = sem("y_out")

        block = ctx.enter_context(nc.Block())

        @block.sync
        def _(sp):
            sp.dma_start(idx[:], ids.rearrange("(t p) f -> p t f", p=P)).then_inc(ids_in, 16)
            sp.dma_start(rows[:, :, 0, :], bottom.rearrange("(t p) d -> p t d", p=P)).then_inc(bottom_in, 16)
            sp.dma_start(w1s[0:KP, 0:CH, :], w_pairs.rearrange("(c k) n -> k c n", k=KP)).then_inc(w1_in, 16)
            sp.dma_start(w1s[:, CH, :], w_bottom).then_inc(w1_in, 16)
            sp.dma_start(w1s[KP:KP + 1, 0, :], b1.rearrange("(a n) -> a n", a=1)).then_inc(w1_in, 16)
            sp.dma_start(w2s[:], w2.rearrange("(c k) n -> k c n", k=P)).then_inc(w2_in, 16)
            sp.dma_start(b2s[:], b2.rearrange("(a n) -> a n", a=1)).then_inc(w2_in, 16)
            sp.dma_start(w3s[:], w3.rearrange("n a -> a n").to_broadcast((P, N2))).then_inc(w3_in, 16)
            for t in range(T):
                sp.wait_ge(y_ok, t + 1)
                sp.dma_start(out[t * P:(t + 1) * P, :], y[:, t:t + 1]).then_inc(y_out, 16)
            sp.wait_ge(y_out, 16 * T)

        @block.gpsimd
        def _(pool):
            nc.gpsimd.memset(ident[:], 0.0).then_inc(ident_zero, 1)
            pool.wait_ge(ident_zero, 1)
            nc.gpsimd.affine_select(out=ident[:], in_=ident[:], compare_op=ALU.not_equal, fill=1.0, base=0,
                                    pattern=[[-1, P]], channel_multiplier=1).then_inc(ident_ok, 1)
            pool.wait_ge(ids_in, 16)
            for t in range(T):
                for g, group in enumerate(GROUPS):
                    for f in group:
                        if f:
                            nc.gpsimd.indirect_dma_start(
                                rows[:, t, f, :], None, tables[f - 1],
                                bass.IndirectOffsetOnAxis(idx[:, t, f - 1:f], 0)).then_inc(rows_in[t][g], 16)

        @block.tensor
        def _(pe):
            def turn(t, g):
                n = t * NG + g
                if g == 0:
                    pe.wait_ge(bottom_in, 16)
                pe.wait_ge(rows_in[t][g], 16 * len([f for f in GROUPS[g] if f]))
                if n >= 2:
                    pe.wait_ge(emb_ok, n - 1)
                for i, f in enumerate(GROUPS[g]):
                    last = nc.tensor.transpose(psT[n % 2][:, i * P:(i + 1) * P], rows[:, t, f, :], ident[:])
                last.then_inc(turned, 1)

            def products(t):
                pe.wait_ge(emb_ok, NG * (t + 1))
                if t == 0:
                    pe.wait_ge(pads_ok, 1)
                else:
                    pe.wait_ge(gram_out, t)
                for q in range(Q):
                    for j in range(BLK):
                        at = (Q * j + q) * F
                        last = nc.tensor.matmul(
                            psG[Q * j:Q * j + Q, q // QB, (q % QB) * F:(q % QB + 1) * F],
                            emb[:, t, at:at + Q], emb[:, t, at:at + F], start=True, stop=True)
                last.then_inc(gram_ok, 1)

            def turn_pairs(t):
                pe.wait_ge(pairs_ok, t + 1)
                if t >= 1:
                    pe.wait_ge(h1t_ok, t)
                for m in range(CH):
                    last = nc.tensor.transpose(psA[0:KP, m * P:(m + 1) * P],
                                               pairs[:, t % 2, m * KP:(m + 1) * KP], ident[:])
                last.then_inc(zt_ps, 1)

            def layer1(t):
                pe.wait_ge(zt_ok, t + 1)
                if t == 0:
                    pe.wait_ge(w1_in, 48)
                else:
                    pe.wait_ge(h2_ok, t)
                bot = emb[:, t, 0:P * F].rearrange("p (b f) -> p f b", f=F)[:, 0, :]
                nc.tensor.matmul(psB[:], bot, w1s[:, CH, :], start=True, stop=False)
                for m in range(CH):
                    k = KP + (m == 0)
                    last = nc.tensor.matmul(psB[:], zt[0:k, t % 2, m, :], w1s[0:k, m, :],
                                            start=False, stop=(m == CH - 1))
                last.then_inc(h1_ps, 1)

            def turn_h1(t):
                pe.wait_ge(h1_ok, t + 1)
                for c in range(K2):
                    last = nc.tensor.transpose(psA[:, c * P:(c + 1) * P], h1[:, t % 2, c * P:(c + 1) * P], ident[:])
                last.then_inc(h1t_ps, 1)

            def layer2(t):
                pe.wait_ge(h1t_ok, t + 1)
                if t == 0:
                    pe.wait_ge(w2_in, 32)
                for c in range(K2):
                    nc.tensor.matmul(psB[:, 0:N2], h1t[:, t % 2, c, :], w2s[:, c, :], start=(c == 0), stop=False)
                nc.tensor.matmul(psB[:, 0:N2], ones[:], b2s[:], start=False, stop=True).then_inc(h2_ps, 1)

            pe.wait_ge(ident_ok, 1)
            for g in range(NG):
                turn(0, g)
            for t in range(T):
                products(t)
                stages = [turn_pairs, layer1, turn_h1, layer2]
                if t + 1 < T:
                    for g in range(NG):
                        turn(t + 1, g)
                        if g < len(stages):
                            stages[g](t)
                else:
                    for stage in stages:
                        stage(t)

        @block.scalar
        def _(act):
            def copy_emb(t, g):
                n = t * NG + g
                act.wait_ge(turned, n + 1)
                group = GROUPS[g]
                dst = emb[:, t, 0:P * F].rearrange("p (b f) -> p f b", f=F)[:, group[0]:group[-1] + 1, :]
                src = psT[n % 2][:, 0:len(group) * P].rearrange("p (f b) -> p f b", b=P)
                nc.scalar.activation(dst, src, ACT.Copy).then_inc(emb_ok, 1)

            def relu1(t):
                act.wait_ge(h1_ps, t + 1)
                if t >= 2:
                    act.wait_ge(h1t_ps, t - 1)
                nc.scalar.activation(h1[:, t % 2, :], psB[:], ACT.Relu).then_inc(h1_ok, 1)

            def relu2(t):
                act.wait_ge(h2_ps, t + 1)
                if t >= 2:
                    act.wait_ge(y_ok, t - 1)
                nc.scalar.activation(h2[:, t % 2, :], psB[:, 0:N2], ACT.Relu).then_inc(h2_ok, 1)

            for g in range(NG):
                copy_emb(0, g)
            for t in range(T):
                after = {1: relu1, 3: relu2}
                for g in range(NG):
                    if t + 1 < T:
                        copy_emb(t + 1, g)
                    if g in after:
                        after[g](t)

        @block.vector
        def _(dve):
            nc.vector.memset(ones[:], 1.0)
            nc.vector.memset(zt[:], 1.0)
            nc.vector.memset(emb[:, :, P * F:P * F + 8], 0.0).then_inc(pads_ok, 1)
            dve.wait_ge(pads_ok, 1)
            for t in range(T):
                dve.wait_ge(gram_ok, t + 1)
                if t >= 2:
                    dve.wait_ge(zt_ps, t - 1)
                src = psG[:, :, 0:QB * F].rearrange("p c (q f) -> p f c q", f=F)
                nc.vector.transpose(gram[:, t % 2, 0:F, :], src).then_inc(gram_out, 1)
                dve.wait_ge(gram_out, t + 1)
                nc.vector.tensor_copy(gram[:, t % 2, F:F + HALF, HALF + 1:F],
                                      gram[:, t % 2, 0:HALF, HALF + 1:F]).then_inc(wrap_ok, 1)
                dve.wait_ge(wrap_ok, t + 1)
                g = gram[:, t % 2]
                cyclic = bass.AP(g.tensor, g.offset + Q, [list(g.ap[0]), [Q, HALF], [Q + 1, F]])
                nc.vector.tensor_copy(pairs[:, t % 2].rearrange("p (s f) -> p s f", f=F),
                                      cyclic).then_inc(pairs_ok, 1)
                dve.wait_ge(zt_ps, t + 1)
                if t >= 2:
                    dve.wait_ge(h1_ps, t - 1)
                nc.vector.tensor_copy(zt[0:KP, t % 2].rearrange("p c b -> p (c b)"),
                                      psA[0:KP, 0:CH * P]).then_inc(zt_ok, 1)
                dve.wait_ge(h1t_ps, t + 1)
                if t >= 2:
                    dve.wait_ge(h2_ps, t - 1)
                nc.vector.tensor_copy(h1t[:, t % 2].rearrange("p c b -> p (c b)"), psA[:]).then_inc(h1t_ok, 1)
                dve.wait_ge(h2_ok, t + 1)
                if t == 0:
                    dve.wait_ge(w3_in, 16)
                nc.vector.tensor_tensor_reduce(prod[:, t % 2, :], h2[:, t % 2, :], w3s[:], 1.0, 0.0,
                                               ALU.mult, ALU.add, y[:, t:t + 1]).then_inc(y_ok, 1)


def kernel(**inputs):
    import numpy as np
    import concourse.bacc as bacc
    from concourse.bass_utils import run_bass_kernel_spmd

    nc = bacc.Bacc("TRN2", target_bir_lowering=False, num_devices=1)
    arrays = {}

    def dram(name, array):
        arrays[name] = np.ascontiguousarray(array)
        return nc.dram_tensor(name, arrays[name].shape, mybir.dt.from_np(arrays[name].dtype),
                              kind="ExternalInput").ap()

    w1 = np.asarray(inputs["W_top1"])
    pairs = pair_order()
    args = [
        dram("bottom", inputs["r_bottom_output"]),
        dram("ids", inputs["ids"]),
        [dram(f"tbl_{i}", inputs[f"tbl_{i}"]) for i in range(TABLES)],
        dram("w_pairs", w1[pairs]),
        dram("w_bottom", w1[len(pairs):]),
        dram("b_top1", inputs["b_top1"]),
        dram("w_top2", inputs["W_top2"]),
        dram("b_top2", inputs["b_top2"]),
        dram("w_top3", inputs["W_top3"]),
    ]
    batch = inputs["ids"].shape[0]
    out = nc.dram_tensor("scores", (batch, 1), F32, kind="ExternalOutput").ap()
    dlrm(nc, *args, out)
    r = run_bass_kernel_spmd(nc, [arrays], core_ids=[0])
    return r.results[0]["scores"]
```

```python
from contextlib import ExitStack

import concourse.bass as bass
from concourse import mybir

ALU = mybir.AluOpType
ACT = mybir.ActivationFunctionType
F32 = mybir.dt.float32
F32R = mybir.dt.float32r
I32 = mybir.dt.int32

P = 128
Q = 32
BLK = P // Q
BANK = 512
TABLES = 26
F = TABLES + 1
HALF = F // 2
PAIRS = HALF * F
CH = 3
KP = PAIRS // CH
GRP = 4
HOT_ROWS = 1000
HOT_TABLES = 8
SUB = 8
ACT_SUB = 2
RAW = 3
IDS = 3
FILL = 4
TILE_OF = [1, 0, 2, 3]
SLOT_OF = [1, 0, 1, 2]


def features(heights):
    hot = [i for i, h in enumerate(heights) if h == HOT_ROWS][:HOT_TABLES]
    cold = [i for i in range(TABLES) if i not in hot]
    return [0] + [i + 1 for i in cold] + [i + 1 for i in hot], 1 + len(cold)


def pair_order(order):
    rows = []
    for step in range(1, HALF + 1):
        for f in range(F):
            lo, hi = sorted((order[f], order[(f + step) % F]))
            rows.append(lo * F - lo * (lo + 1) // 2 + hi - lo - 1)
    return rows


ORDER = [
    ("hot", 0), ("turn", 0, 0), ("hot", 1), ("turn", 0, 1), ("hot", 2), ("hot", 3), ("turn", 0, 2),
    ("hot", 4), ("turn", 0, 3), ("hot", 5), ("turn", 0, 4), ("hot", 6), ("turn", 1, 0), ("hot", 7),
    ("products", 0), ("turn", 1, 1), ("hot", 8), ("pairs", 0), ("turn", 1, 2), ("layer1", 0),
    ("turn", 1, 3), ("hidden", 0), ("hot", 9), ("layer2", 0), ("turn", 1, 4), ("hot", 10),
    ("products", 1), ("turn", 2, 0), ("turn", 2, 1), ("hot", 11), ("pairs", 1), ("hot", 12),
    ("layer1", 1), ("turn", 2, 2), ("hidden", 1), ("turn", 2, 3), ("layer2", 1), ("turn", 2, 4),
    ("hot", 13), ("hot", 14), ("turn", 3, 0), ("hot", 15), ("turn", 3, 1), ("products", 2),
    ("turn", 3, 2), ("pairs", 2), ("layer1", 2), ("turn", 3, 3), ("hidden", 2), ("turn", 3, 4),
    ("layer2", 2), ("products", 3), ("pairs", 3), ("layer1", 3), ("hidden", 3), ("layer2", 3),
]


def dlrm(nc, bottom, ids, ids_hot, tables, w_pairs, w_bottom, b1, w2, b2, w3, out):
    B, D = bottom.shape
    N1 = w_pairs.shape[1]
    N2 = w2.shape[1]
    T = B // P
    HB = B // 2
    K2 = N1 // P
    FEATS, COLD = features([t.shape[0] for t in tables])
    HOT = F - COLD
    UNITS = 2 * HOT
    GROUPS = [range(f, min(f + GRP, COLD)) for f in range(0, COLD, GRP)]
    NG = len(GROUPS)
    QB = Q // 2
    FULL = (SUB - 1) * P
    REST = HOT_ROWS - FULL
    SPAN = P * F + 8
    fills = [step for step in ORDER if step[0] in ("hot", "turn")]
    NTH = {step: n for n, step in enumerate(fills)}

    with ExitStack() as ctx:
        def sb(name, shape, dt=F32):
            return ctx.enter_context(nc.sbuf_tensor(name, shape, dt))

        def ps(name, shape):
            return ctx.enter_context(nc.psum_tensor(name, shape, F32))

        def sem(name):
            return ctx.enter_context(nc.semaphore(name))

        idx = sb("idx", [P, T, TABLES], I32)
        bot = sb("bot", [P, T, D])
        rows = sb("rows", [P, 2, COLD - 1, D])
        ident = sb("ident", [P, P])
        emb = sb("emb", [P, 3, SPAN])
        raw = sb("raw", [P, RAW, SUB, D])
        hot_hi = sb("hot_hi", [P, HOT, SUB, D], F32R)
        hot_lo = sb("hot_lo", [P, HOT, SUB, D], F32R)
        spread = sb("spread", [P, IDS, HB], I32)
        row_id = sb("row_id", [P, SUB])
        row_neg = sb("row_neg", [P, SUB])
        apart = sb("apart", [P, ACT_SUB, HB])
        onehot = sb("onehot", [P, 2, SUB, HB], F32R)
        gram = sb("gram", [P, F + HALF, Q])
        pairs = sb("pairs", [P, PAIRS])
        z_hi = sb("z_hi", [P, CH, P], F32R)
        z_lo = sb("z_lo", [P, CH, P], F32R)
        h1 = sb("h1", [P, N1])
        h1_hi = sb("h1_hi", [P, K2, P], F32R)
        h1_lo = sb("h1_lo", [P, K2, P], F32R)
        h2 = sb("h2", [P, N2])
        prod = sb("prod", [P, N2])
        y = sb("y", [P, T])
        scrap = sb("scrap", [P, 1])
        wb = sb("wb", [P, N1])
        w1_hi = sb("w1_hi", [P, CH, N1], F32R)
        w1_lo = sb("w1_lo", [P, CH, N1], F32R)
        w2_hi = sb("w2_hi", [P, K2, N2], F32R)
        w2_lo = sb("w2_lo", [P, K2, N2], F32R)
        w3s = sb("w3s", [P, N2])
        b2s = sb("b2s", [1, N2])
        ones = sb("ones", [1, P])
        assert HOT % RAW == 2 and CH * N1 <= 2 * SUB * D and K2 * N2 <= SUB * D
        w1_raw = raw[:].rearrange("p r k d -> p (r k d)")[:, 0:CH * N1]
        w2_raw = raw[:, RAW - 1].rearrange("p k d -> p (k d)")[:, 0:K2 * N2]

        psF = [ps(f"psF{i}", [P, BANK]) for i in range(FILL)]
        psG = ps("psG", [P, 2, BANK])
        psA = ps("psA", [P, BANK])
        psB = ps("psB", [P, BANK])

        ids_in = sem("ids_in")
        bottom_in = sem("bottom_in")
        raw_in = [sem(f"raw_in_{k}") for k in range(HOT)]
        spread_in = [sem(f"spread_in_{i}") for i in range(IDS)]
        w1_in = sem("w1_in")
        w2_in = sem("w2_in")
        wb_in = sem("wb_in")
        w3_in = sem("w3_in")
        rows_in = [[sem(f"rows_in_{s}_{g}") for g in range(NG)] for s in range(T)]
        ident_zero = sem("ident_zero")
        ident_ok = sem("ident_ok")
        ids_ok = sem("ids_ok")
        neg_ok = sem("neg_ok")
        set_ok = sem("set_ok")
        raw_clear = sem("raw_clear")
        hi_ok = sem("hi_ok")
        lo_ok = sem("lo_ok")
        w1_hi_ok = sem("w1_hi_ok")
        w1_lo_ok = sem("w1_lo_ok")
        w2_hi_ok = sem("w2_hi_ok")
        w2_lo_ok = sem("w2_lo_ok")
        apart_ok = sem("apart_ok")
        act_cols = sem("act_cols")
        dve_cols = sem("dve_cols")
        filled = sem("filled")
        emptied = sem("emptied")
        gram_ok = sem("gram_ok")
        gram_out = sem("gram_out")
        wrap_ok = sem("wrap_ok")
        pairs_ok = sem("pairs_ok")
        z_ps = sem("z_ps")
        z_hi_ok = sem("z_hi_ok")
        z_lo_ok = sem("z_lo_ok")
        h1_ps = sem("h1_ps")
        h1_ok = sem("h1_ok")
        h1t_ps = sem("h1t_ps")
        h1_hi_ok = sem("h1_hi_ok")
        h1_lo_ok = sem("h1_lo_ok")
        h2_ps = sem("h2_ps")
        h2_ok = sem("h2_ok")
        y_ok = sem("y_ok")
        y_out = sem("y_out")

        block = ctx.enter_context(nc.Block())

        @block.sync
        def _(sp):
            def load_table(k):
                if k >= RAW:
                    sp.wait_ge(lo_ok, k - RAW + 1)
                table = tables[FEATS[COLD + k] - 1]
                sp.dma_start(raw[:, k % RAW, 0:SUB - 1, :],
                             table[0:FULL, :].rearrange("(p k) d -> p k d", k=SUB - 1)).then_inc(raw_in[k], 16)
                if k < RAW:
                    sp.wait_ge(raw_clear, 1)
                sp.dma_start(raw[0:REST, k % RAW, SUB - 1, :], table[FULL:HOT_ROWS, :]).then_inc(raw_in[k], 16)

            def load_ids(u):
                if u >= IDS:
                    sp.wait_ge(act_cols, u - IDS + 1)
                    sp.wait_ge(dve_cols, u - IDS + 1)
                h, k = divmod(u, HOT)
                sp.dma_start(spread[:, u % IDS, :],
                             ids_hot[k:k + 1, h * HB:(h + 1) * HB].to_broadcast((P, HB))).then_inc(spread_in[u % IDS], 16)

            sp.dma_start(idx[:], ids.rearrange("(t p) f -> p t f", p=P)).then_inc(ids_in, 16)
            load_table(0)
            load_table(1)
            sp.dma_start(bot[:], bottom.rearrange("(t p) d -> p t d", p=P)).then_inc(bottom_in, 16)
            for k in range(2, HOT):
                load_table(k)
                if k >= IDS:
                    load_ids(k)
            load_ids(HOT)
            sp.wait_ge(lo_ok, HOT - 2)
            sp.dma_start(w2_raw.rearrange("p (c n) -> p c n", n=N2),
                         w2.rearrange("(c k) n -> k c n", k=P)).then_inc(w2_in, 16)
            load_ids(HOT + 1)
            sp.wait_ge(lo_ok, HOT)
            sp.dma_start(w1_raw[0:KP, :].rearrange("p (c n) -> p c n", n=N1),
                         w_pairs.rearrange("(c k) n -> k c n", k=KP)).then_inc(w1_in, 16)
            sp.dma_start(w1_raw[KP:KP + 1, 0:N1], b1.rearrange("(a n) -> a n", a=1)).then_inc(w1_in, 16)
            sp.dma_start(wb[:], w_bottom).then_inc(wb_in, 16)
            sp.dma_start(b2s[:], b2.rearrange("(a n) -> a n", a=1)).then_inc(wb_in, 16)
            sp.dma_start(w3s[:], w3.rearrange("n a -> a n").to_broadcast((P, N2))).then_inc(w3_in, 16)
            for u in range(HOT + 2, UNITS):
                load_ids(u)
            for s in range(T):
                t = TILE_OF[s]
                sp.wait_ge(y_ok, s + 1)
                sp.dma_start(out[t * P:(t + 1) * P, :], y[:, t:t + 1]).then_inc(y_out, 16)
            sp.wait_ge(y_out, 16 * T)

        @block.gpsimd
        def _(pool):
            nc.gpsimd.iota(row_id[:, 0:SUB - 1], [[1, SUB - 1]], base=0, channel_multiplier=SUB - 1,
                           allow_small_or_imprecise_dtypes=True).then_inc(ids_ok, 1)
            nc.gpsimd.iota(row_id[:, SUB - 1:SUB], [[1, 1]], base=FULL, channel_multiplier=1,
                           allow_small_or_imprecise_dtypes=True).then_inc(ids_ok, 1)
            nc.gpsimd.memset(ident[:], 0.0).then_inc(ident_zero, 1)
            pool.wait_ge(ident_zero, 1)
            nc.gpsimd.affine_select(out=ident[:], in_=ident[:], compare_op=ALU.not_equal, fill=1.0, base=0,
                                    pattern=[[-1, P]], channel_multiplier=1).then_inc(ident_ok, 1)
            pool.wait_ge(ids_in, 16)
            for s in range(T):
                for g, group in enumerate(GROUPS):
                    if s >= 2:
                        pool.wait_ge(filled, NTH["turn", s - 2, g] + 1)
                    for f in group:
                        if f:
                            table = FEATS[f] - 1
                            nc.gpsimd.indirect_dma_start(
                                rows[:, s % 2, f - 1, :], None, tables[table],
                                bass.IndirectOffsetOnAxis(idx[:, TILE_OF[s], table:table + 1], 0)
                            ).then_inc(rows_in[s][g], 16)

        @block.tensor
        def _(pe):
            pe.wait_ge(ident_ok, 1)
            for step in ORDER:
                name, s = step[0], step[1]
                if name in ("hot", "turn"):
                    n = NTH[step]
                    if n >= FILL:
                        pe.wait_ge(emptied, n - FILL + 1)
                if name == "hot":
                    u = s
                    h, k = divmod(u, HOT)
                    if h == 0:
                        pe.wait_ge(hi_ok, k + 1)
                        pe.wait_ge(lo_ok, k + 1)
                    pe.wait_ge(act_cols, u + 1)
                    pe.wait_ge(dve_cols, u + 1)
                    for b in range(SUB):
                        kr = P if b < SUB - 1 else REST
                        for part in (hot_hi, hot_lo):
                            last = nc.tensor.matmul(psF[n % FILL][:, 0:HB], part[0:kr, k, b, :],
                                                    onehot[0:kr, u % 2, b, :],
                                                    start=(b == 0 and part is hot_hi),
                                                    stop=(b == SUB - 1 and part is hot_lo))
                    last.then_inc(filled, 1)
                elif name == "turn":
                    g = step[2]
                    if g == 0:
                        pe.wait_ge(bottom_in, 16)
                    pe.wait_ge(rows_in[s][g], 16 * len([f for f in GROUPS[g] if f]))
                    for i, f in enumerate(GROUPS[g]):
                        src = rows[:, s % 2, f - 1, :] if f else bot[:, TILE_OF[s], :]
                        last = nc.tensor.transpose(psF[n % FILL][:, i * P:(i + 1) * P], src, ident[:])
                    last.then_inc(filled, 1)
                elif name == "products":
                    pe.wait_ge(emptied, max(NTH["turn", s, NG - 1], NTH["hot", HOT * (1 + s // 2) - 1]) + 1)
                    pe.wait_ge(set_ok, 1)
                    if s >= 1:
                        pe.wait_ge(gram_out, s)
                    slot = SLOT_OF[s]
                    wide = Q
                    for q in range(Q):
                        for j in range(BLK):
                            at = (Q * j + q) * F
                            last = nc.tensor.matmul(
                                psG[Q * j:Q * j + Q, q // QB, (q % QB) * Q:(q % QB) * Q + wide],
                                emb[:, slot, at:at + Q], emb[:, slot, at:at + wide], start=True, stop=True)
                    last.then_inc(gram_ok, 1)
                elif name == "pairs":
                    pe.wait_ge(pairs_ok, s + 1)
                    if s >= 1:
                        pe.wait_ge(h1_lo_ok, s)
                    for m in range(CH):
                        last = nc.tensor.transpose(psA[0:KP, m * P:(m + 1) * P],
                                                   pairs[:, m * KP:(m + 1) * KP], ident[:])
                    last.then_inc(z_ps, 1)
                elif name == "layer1":
                    if s == 0:
                        pe.wait_ge(w1_hi_ok, 1)
                        pe.wait_ge(w1_lo_ok, 1)
                        pe.wait_ge(wb_in, 32)
                    else:
                        pe.wait_ge(h2_ok, s)
                    x = emb[:, SLOT_OF[s], 0:P * F].rearrange("p (b f) -> p f b", f=F)[:, 0, :]
                    nc.tensor.matmul(psB[:], x, wb[:], start=True, stop=False)
                    pe.wait_ge(z_hi_ok, s + 1)
                    for m in range(CH):
                        kr = KP + (m == 0)
                        nc.tensor.matmul(psB[:], z_hi[0:kr, m, :], w1_hi[0:kr, m, :], start=False, stop=False)
                        nc.tensor.matmul(psB[:], z_hi[0:kr, m, :], w1_lo[0:kr, m, :], start=False, stop=False)
                    pe.wait_ge(z_lo_ok, s + 1)
                    for m in range(CH):
                        last = nc.tensor.matmul(psB[:], z_lo[0:KP, m, :], w1_hi[0:KP, m, :],
                                                start=False, stop=(m == CH - 1))
                    last.then_inc(h1_ps, 1)
                elif name == "hidden":
                    pe.wait_ge(h1_ok, s + 1)
                    for c in range(K2):
                        last = nc.tensor.transpose(psA[:, c * P:(c + 1) * P], h1[:, c * P:(c + 1) * P], ident[:])
                    last.then_inc(h1t_ps, 1)
                elif name == "layer2":
                    if s == 0:
                        pe.wait_ge(w2_hi_ok, 1)
                        pe.wait_ge(w2_lo_ok, 1)
                    nc.tensor.matmul(psB[:, 0:N2], ones[:], b2s[:], start=True, stop=False)
                    pe.wait_ge(h1_hi_ok, s + 1)
                    for c in range(K2):
                        nc.tensor.matmul(psB[:, 0:N2], h1_hi[:, c, :], w2_hi[:, c, :], start=False, stop=False)
                        nc.tensor.matmul(psB[:, 0:N2], h1_hi[:, c, :], w2_lo[:, c, :], start=False, stop=False)
                    pe.wait_ge(h1_lo_ok, s + 1)
                    for c in range(K2):
                        last = nc.tensor.matmul(psB[:, 0:N2], h1_lo[:, c, :], w2_hi[:, c, :],
                                                start=False, stop=(c == K2 - 1))
                    last.then_inc(h2_ps, 1)

        @block.scalar
        def _(act):
            def table_hi(k):
                act.wait_ge(raw_in[k], 32)
                nc.scalar.activation(hot_hi[:, k], raw[:, k % RAW], ACT.Copy).then_inc(hi_ok, 1)

            def columns(u):
                act.wait_ge(spread_in[u % IDS], 16 * (u // IDS + 1))
                if u >= 1:
                    act.wait_ge(act_cols, u)
                for b in range(ACT_SUB):
                    last = nc.scalar.activation(apart[:, b, :], spread[:, u % IDS, :], ACT.Abs,
                                                bias=row_neg[:, b:b + 1])
                last.then_inc(apart_ok, 1)
                act.wait_ge(apart_ok, u + 1)
                if u >= 2:
                    act.wait_ge(filled, NTH["hot", u - 2] + 1)
                nc.scalar.activation(onehot[:, u % 2, 0:ACT_SUB, :], apart[:], ACT.Relu,
                                     bias=1.0, scale=-1.0).then_inc(act_cols, 1)

            for u in range(IDS):
                act.dma_start(spread[:, u % IDS, :],
                              ids_hot[u:u + 1, 0:HB].to_broadcast((P, HB))).then_inc(spread_in[u % IDS], 16)
            act.wait_ge(neg_ok, 1)
            nc.scalar.activation(scrap[:], row_neg[:, 0:1], ACT.Abs)
            columns(0)
            table_hi(0)
            table_hi(1)
            for step in ORDER:
                name, s = step[0], step[1]
                if name in ("hot", "turn"):
                    if name == "hot" and s + 1 < UNITS:
                        if s + 2 < HOT:
                            table_hi(s + 2)
                        columns(s + 1)
                    n = NTH[step]
                    act.wait_ge(filled, n + 1)
                if name == "hot":
                    h, k = divmod(s, HOT)
                    if h == 1:
                        act.wait_ge(gram_ok, 1)
                    dst = emb[:, h:h + 2, 0:P * F].rearrange("p t (b f) -> p f t b", f=F)[:, COLD + k]
                    src = psF[n % FILL][:, 0:HB].rearrange("p (t b) -> p t b", b=P)
                    nc.scalar.activation(dst, src, ACT.Copy).then_inc(emptied, 1)
                    if s == HOT - 1:
                        act.wait_ge(w2_in, 16)
                        nc.scalar.activation(w2_hi[:].rearrange("p c n -> p (c n)"), w2_raw,
                                             ACT.Copy).then_inc(w2_hi_ok, 1)
                elif name == "turn":
                    group = GROUPS[step[2]]
                    if s == 2:
                        act.wait_ge(gram_ok, 1)
                    dst = emb[:, SLOT_OF[s], 0:P * F].rearrange("p (b f) -> p f b", f=F)
                    src = psF[n % FILL][:, 0:len(group) * P].rearrange("p (f b) -> p f b", b=P)
                    nc.scalar.activation(dst[:, group[0]:group[-1] + 1, :], src, ACT.Copy).then_inc(emptied, 1)
                elif name == "products" and s == 0:
                    act.wait_ge(w1_in, 32)
                    nc.scalar.activation(w1_hi[0:KP + 1, 0, :], w1_raw[0:KP + 1, 0:N1], ACT.Copy)
                    nc.scalar.activation(w1_hi[0:KP, 1:CH, :].rearrange("p c n -> p (c n)"),
                                         w1_raw[0:KP, N1:CH * N1], ACT.Copy).then_inc(w1_hi_ok, 1)
                elif name == "pairs":
                    act.wait_ge(z_ps, s + 1)
                    if s >= 1:
                        act.wait_ge(h1_ps, s)
                    nc.scalar.activation(z_hi[0:KP].rearrange("p c b -> p (c b)"), psA[0:KP, 0:CH * P],
                                         ACT.Copy).then_inc(z_hi_ok, 1)
                elif name == "layer1":
                    act.wait_ge(h1_ps, s + 1)
                    if s >= 1:
                        act.wait_ge(h1t_ps, s)
                    nc.scalar.activation(h1[:], psB[:], ACT.Relu).then_inc(h1_ok, 1)
                elif name == "hidden":
                    act.wait_ge(h1t_ps, s + 1)
                    if s >= 1:
                        act.wait_ge(h2_ps, s)
                    nc.scalar.activation(h1_hi[:].rearrange("p c b -> p (c b)"), psA[:], ACT.Copy).then_inc(h1_hi_ok, 1)
                elif name == "layer2":
                    act.wait_ge(h2_ps, s + 1)
                    if s >= 1:
                        act.wait_ge(y_ok, s)
                    nc.scalar.activation(h2[:], psB[:, 0:N2], ACT.Relu).then_inc(h2_ok, 1)

        @block.vector
        def _(dve):
            def table_lo(k):
                dve.wait_ge(hi_ok, k + 1)
                nc.vector.tensor_tensor(hot_lo[:, k], raw[:, k % RAW], hot_hi[:, k].bitcast(F32),
                                        ALU.subtract).then_inc(lo_ok, 1)

            def columns(u):
                dve.wait_ge(spread_in[u % IDS], 16 * (u // IDS + 1))
                if u >= 2:
                    dve.wait_ge(filled, NTH["hot", u - 2] + 1)
                own = SUB - ACT_SUB
                src = spread[:, u % IDS, :]
                row = row_id[:, ACT_SUB:SUB]
                nc.vector.tensor_tensor(onehot[:, u % 2, ACT_SUB:SUB, :],
                                        bass.AP(src.tensor, src.offset, [list(src.ap[0]), [0, own], [1, HB]]),
                                        bass.AP(row.tensor, row.offset, [list(row.ap[0]), [1, own], [0, HB]]),
                                        ALU.is_equal).then_inc(dve_cols, 1)

            nc.vector.memset(raw[P - Q:P, :, SUB - 1, :], 0.0).then_inc(raw_clear, 1)
            dve.wait_ge(ids_ok, 2)
            nc.vector.tensor_scalar(row_neg[:], row_id[:], -1.0, None, ALU.mult).then_inc(neg_ok, 1)
            columns(0)
            nc.vector.memset(ones[:], 1.0)
            nc.vector.memset(z_hi[:].bitcast(F32), 1.0)
            nc.vector.memset(z_lo[:].bitcast(F32), 0.0)
            nc.vector.memset(emb[:, :, P * F:SPAN], 0.0).then_inc(set_ok, 1)
            table_lo(0)
            for step in ORDER:
                name, s = step[0], step[1]
                if name == "hot" and s + 1 < UNITS:
                    columns(s + 1)
                    if s + 1 < HOT:
                        table_lo(s + 1)
                    if s == HOT - 1:
                        dve.wait_ge(w2_hi_ok, 1)
                        nc.vector.tensor_tensor(w2_lo[:].rearrange("p c n -> p (c n)"), w2_raw,
                                                w2_hi[:].rearrange("p c n -> p (c n)").bitcast(F32),
                                                ALU.subtract).then_inc(w2_lo_ok, 1)
                elif name == "products":
                    if s == 0:
                        dve.wait_ge(w1_hi_ok, 1)
                        nc.vector.tensor_tensor(w1_lo[0:KP + 1, 0, :], w1_raw[0:KP + 1, 0:N1],
                                                w1_hi[0:KP + 1, 0, :].bitcast(F32), ALU.subtract)
                        nc.vector.tensor_tensor(w1_lo[0:KP, 1:CH, :].rearrange("p c n -> p (c n)"),
                                                w1_raw[0:KP, N1:CH * N1],
                                                w1_hi[0:KP, 1:CH, :].rearrange("p c n -> p (c n)").bitcast(F32),
                                                ALU.subtract).then_inc(w1_lo_ok, 1)
                    dve.wait_ge(gram_ok, s + 1)
                    src = psG[:].rearrange("p c (q f) -> p f c q", f=Q)[:, 0:F]
                    nc.vector.transpose(gram[:, 0:F, :], src).then_inc(gram_out, 1)
                    dve.wait_ge(gram_out, s + 1)
                    nc.vector.tensor_copy(gram[:, F:F + HALF, HALF + 1:F],
                                          gram[:, 0:HALF, HALF + 1:F]).then_inc(wrap_ok, 1)
                    dve.wait_ge(wrap_ok, s + 1)
                    if s >= 1:
                        dve.wait_ge(z_ps, s)
                    g = gram[:]
                    cyclic = bass.AP(g.tensor, g.offset + Q, [list(g.ap[0]), [Q, HALF], [Q + 1, F]])
                    nc.vector.tensor_copy(pairs[:].rearrange("p (s f) -> p s f", f=F), cyclic).then_inc(pairs_ok, 1)
                elif name == "pairs":
                    dve.wait_ge(z_hi_ok, s + 1)
                    if s >= 1:
                        dve.wait_ge(h1_ps, s)
                    nc.vector.tensor_tensor(z_lo[0:KP].rearrange("p c b -> p (c b)"), psA[0:KP, 0:CH * P],
                                            z_hi[0:KP].rearrange("p c b -> p (c b)").bitcast(F32),
                                            ALU.subtract).then_inc(z_lo_ok, 1)
                elif name == "hidden":
                    dve.wait_ge(h1_hi_ok, s + 1)
                    if s >= 1:
                        dve.wait_ge(h2_ps, s)
                    nc.vector.tensor_tensor(h1_lo[:].rearrange("p c b -> p (c b)"), psA[:],
                                            h1_hi[:].rearrange("p c b -> p (c b)").bitcast(F32),
                                            ALU.subtract).then_inc(h1_lo_ok, 1)
                elif name == "layer2":
                    dve.wait_ge(h2_ok, s + 1)
                    if s == 0:
                        dve.wait_ge(w3_in, 16)
                    t = TILE_OF[s]
                    nc.vector.tensor_tensor_reduce(prod[:], h2[:], w3s[:], 1.0, 0.0,
                                                   ALU.mult, ALU.add, y[:, t:t + 1]).then_inc(y_ok, 1)


def kernel(**inputs):
    import numpy as np
    import concourse.bacc as bacc
    from concourse.bass_utils import run_bass_kernel_spmd

    nc = bacc.Bacc("TRN2", target_bir_lowering=False, num_devices=1)
    arrays = {}

    def dram(name, array):
        arrays[name] = np.ascontiguousarray(array)
        return nc.dram_tensor(name, arrays[name].shape, mybir.dt.from_np(arrays[name].dtype),
                              kind="ExternalInput").ap()

    order, cold = features([inputs[f"tbl_{i}"].shape[0] for i in range(TABLES)])
    w1 = np.asarray(inputs["W_top1"])
    ids = np.asarray(inputs["ids"])
    args = [
        dram("bottom", inputs["r_bottom_output"]),
        dram("ids", ids),
        dram("ids_hot", ids[:, [f - 1 for f in order[cold:]]].T),
        [dram(f"tbl_{i}", inputs[f"tbl_{i}"]) for i in range(TABLES)],
        dram("w_pairs", w1[pair_order(order)]),
        dram("w_bottom", w1[PAIRS:]),
        dram("b_top1", inputs["b_top1"]),
        dram("w_top2", inputs["W_top2"]),
        dram("b_top2", inputs["b_top2"]),
        dram("w_top3", inputs["W_top3"]),
    ]
    out = nc.dram_tensor("scores", (ids.shape[0], 1), F32, kind="ExternalOutput").ap()
    dlrm(nc, *args, out)
    r = run_bass_kernel_spmd(nc, [arrays], core_ids=[0])
    return r.results[0]["scores"]
```

```python
from contextlib import ExitStack

import concourse.bass as bass
from concourse import mybir

ALU = mybir.AluOpType
ACT = mybir.ActivationFunctionType
F32 = mybir.dt.float32
F32R = mybir.dt.float32r
I32 = mybir.dt.int32

P = 128
Q = 32
BLK = P // Q
BANK = 512
TABLES = 26
F = TABLES + 1
HALF = F // 2
PAIRS = HALF * F
CH = 3
KP = PAIRS // CH
GRP = 4
HOT_ROWS = 1000
HOT_TABLES = 8
SUB = 8
ACT_SUB = 1
RAW = 3
IDS = 3
FILL = 4
TILE_OF = [1, 0, 2, 3]
SLOT_OF = [1, 0, 1, 2]


def features(heights):
    hot = [i for i, h in enumerate(heights) if h == HOT_ROWS][:HOT_TABLES]
    cold = [i for i in range(TABLES) if i not in hot]
    return [0] + [i + 1 for i in cold] + [i + 1 for i in hot], 1 + len(cold)


def pair_order(order):
    rows = []
    for step in range(1, HALF + 1):
        for f in range(F):
            lo, hi = sorted((order[f], order[(f + step) % F]))
            rows.append(lo * F - lo * (lo + 1) // 2 + hi - lo - 1)
    return rows


ORDER = [
    ("hot", 0), ("turn", 0, 0), ("hot", 1), ("hot", 2), ("turn", 0, 1), ("hot", 3), ("hot", 4),
    ("hot", 5), ("turn", 0, 2), ("hot", 6), ("turn", 0, 3), ("turn", 0, 4), ("turn", 0, 5), ("hot", 7),
    ("turn", 1, 0), ("turn", 1, 1), ("products", 0), ("turn", 1, 2), ("hot", 8), ("pairs", 0),
    ("layer1", 0), ("hot", 9), ("turn", 1, 3), ("turn", 1, 4), ("turn", 1, 5), ("hidden", 0),
    ("turn", 2, 0), ("hot", 10), ("products", 1), ("turn", 2, 1), ("hot", 11), ("layer2", 0),
    ("pairs", 1), ("turn", 2, 2), ("layer1", 1), ("hot", 12), ("turn", 2, 3), ("turn", 2, 4),
    ("turn", 2, 5), ("hot", 13), ("hot", 14), ("hidden", 1), ("hot", 15), ("turn", 3, 0),
    ("products", 2), ("turn", 3, 1), ("layer2", 1), ("turn", 3, 2), ("pairs", 2), ("layer1", 2),
    ("turn", 3, 3), ("turn", 3, 4), ("turn", 3, 5), ("hidden", 2), ("products", 3), ("layer2", 2),
    ("pairs", 3), ("layer1", 3), ("hidden", 3), ("layer2", 3),
]


def dlrm(nc, bottom, ids, ids_hot, tables, w_pairs, w_bottom, b1, w2, b2, w3, out):
    B, D = bottom.shape
    N1 = w_pairs.shape[1]
    N2 = w2.shape[1]
    T = B // P
    HB = B // 2
    K2 = N1 // P
    FEATS, COLD = features([t.shape[0] for t in tables])
    HOT = F - COLD
    UNITS = 2 * HOT
    GROUPS = [range(f, min(f + GRP, COLD - 1)) for f in range(0, COLD - 1, GRP)] + [range(COLD - 1, COLD)]
    NG = len(GROUPS)
    QB = Q // 2
    FULL = (SUB - 1) * P
    REST = HOT_ROWS - FULL
    SPAN = P * F + Q - F
    fills = [step for step in ORDER if step[0] in ("hot", "turn")]
    NTH = {step: n for n, step in enumerate(fills)}

    with ExitStack() as ctx:
        def sb(name, shape, dt=F32):
            return ctx.enter_context(nc.sbuf_tensor(name, shape, dt))

        def ps(name, shape):
            return ctx.enter_context(nc.psum_tensor(name, shape, F32))

        def sem(name):
            return ctx.enter_context(nc.semaphore(name))

        idx = sb("idx", [P, T, TABLES], I32)
        bot = sb("bot", [P, T, D])
        rows = sb("rows", [P, 2, COLD - 1, D])
        ident = sb("ident", [P, P])
        emb = sb("emb", [P, 3, SPAN])
        raw = sb("raw", [P, RAW, SUB, D])
        hot_hi = sb("hot_hi", [P, HOT, SUB, D], F32R)
        hot_lo = sb("hot_lo", [P, HOT, SUB, D], F32R)
        spread = sb("spread", [P, IDS, HB], I32)
        row_id = sb("row_id", [P, SUB])
        row_neg = sb("row_neg", [P, SUB])
        apart = sb("apart", [P, ACT_SUB, HB])
        onehot = sb("onehot", [P, 2, SUB, HB], F32R)
        gram = sb("gram", [P, F + HALF, Q])
        pairs = sb("pairs", [P, PAIRS])
        z_hi = sb("z_hi", [P, CH, P], F32R)
        z_lo = sb("z_lo", [P, CH, P], F32R)
        h1 = sb("h1", [P, N1])
        h1_hi = sb("h1_hi", [P, K2, P], F32R)
        h1_lo = sb("h1_lo", [P, K2, P], F32R)
        weighed = sb("weighed", [P, N2])
        y = sb("y", [P, T])
        scrap = sb("scrap", [P, 2])
        wb = sb("wb", [P, N1])
        w1_hi = sb("w1_hi", [P, CH, N1], F32R)
        w1_lo = sb("w1_lo", [P, CH, N1], F32R)
        w2_hi = sb("w2_hi", [P, K2, N2], F32R)
        w2_lo = sb("w2_lo", [P, K2, N2], F32R)
        w3s = sb("w3s", [P, N2])
        b2_raw = sb("b2_raw", [Q + 1, N2])
        b2_split = sb("b2_split", [Q + 1, N2], F32R)
        ones = sb("ones", [Q + 1, P], F32R)
        assert CH * N1 + K2 * N2 <= P * F
        w1_raw = emb[:, 2, 0:CH * N1]
        w2_raw = emb[:, 2, CH * N1:CH * N1 + K2 * N2]

        psF = [ps(f"psF{i}", [P, BANK]) for i in range(FILL)]
        psG = ps("psG", [P, 2, BANK])
        psA = ps("psA", [P, BANK])
        psB = ps("psB", [P, BANK])

        ids_in = sem("ids_in")
        bottom_in = sem("bottom_in")
        raw_in = [sem(f"raw_in_{k}") for k in range(HOT)]
        spread_in = [sem(f"spread_in_{i}") for i in range(IDS)]
        w1_in = sem("w1_in")
        w2_in = sem("w2_in")
        wb_in = sem("wb_in")
        b2_clear = sem("b2_clear")
        b2_in = sem("b2_in")
        b2_hi_ok = sem("b2_hi_ok")
        b2_ok = sem("b2_ok")
        w3_in = sem("w3_in")
        rows_in = [[sem(f"rows_in_{s}_{g}") for g in range(NG)] for s in range(T)]
        ident_zero = sem("ident_zero")
        ident_ok = sem("ident_ok")
        ids_ok = sem("ids_ok")
        neg_ok = sem("neg_ok")
        scrap_ok = sem("scrap_ok")
        set_ok = sem("set_ok")
        raw_clear = sem("raw_clear")
        hi_ok = sem("hi_ok")
        lo_ok = sem("lo_ok")
        w1_hi_ok = sem("w1_hi_ok")
        w1_lo_ok = sem("w1_lo_ok")
        w2_hi_ok = sem("w2_hi_ok")
        w2_lo_ok = sem("w2_lo_ok")
        apart_ok = sem("apart_ok")
        act_cols = sem("act_cols")
        dve_cols = sem("dve_cols")
        filled = sem("filled")
        emptied = sem("emptied")
        gram_ok = sem("gram_ok")
        gram_out = sem("gram_out")
        wrap_ok = sem("wrap_ok")
        pairs_ok = sem("pairs_ok")
        z_ps = sem("z_ps")
        z_hi_ok = sem("z_hi_ok")
        z_lo_ok = sem("z_lo_ok")
        h1_ps = sem("h1_ps")
        h1_ok = sem("h1_ok")
        h1t_ps = sem("h1t_ps")
        h1_hi_ok = sem("h1_hi_ok")
        h1_lo_ok = sem("h1_lo_ok")
        h2_ps = sem("h2_ps")
        y_ok = sem("y_ok")
        y_out = sem("y_out")

        block = ctx.enter_context(nc.Block())

        @block.sync
        def _(sp):
            def load_table(k):
                if k >= RAW:
                    sp.wait_ge(lo_ok, k - RAW + 1)
                table = tables[FEATS[COLD + k] - 1]
                sp.dma_start(raw[:, k % RAW, 0:SUB - 1, :],
                             table[0:FULL, :].rearrange("(p k) d -> p k d", k=SUB - 1)).then_inc(raw_in[k], 16)
                if k < RAW:
                    sp.wait_ge(raw_clear, 1)
                sp.dma_start(raw[0:REST, k % RAW, SUB - 1, :], table[FULL:HOT_ROWS, :]).then_inc(raw_in[k], 16)

            def load_ids(u):
                if u >= IDS:
                    sp.wait_ge(act_cols, u - IDS + 1)
                    sp.wait_ge(dve_cols, u - IDS + 1)
                h, k = divmod(u, HOT)
                sp.dma_start(
                    spread[:, u % IDS, :],
                    ids_hot[k:k + 1, h * HB:(h + 1) * HB].to_broadcast((P, HB))).then_inc(spread_in[u % IDS], 16)

            sp.dma_start(idx[:], ids.rearrange("(t p) f -> p t f", p=P)).then_inc(ids_in, 16)
            load_ids(0)
            load_table(0)
            load_table(1)
            sp.dma_start(bot[:], bottom.rearrange("(t p) d -> p t d", p=P)).then_inc(bottom_in, 16)
            for k in range(2, HOT):
                if k >= IDS:
                    load_ids(k)
                load_table(k)
            sp.dma_start(w1_raw[0:KP, :].rearrange("p (c n) -> p c n", n=N1),
                         w_pairs.rearrange("(c k) n -> k c n", k=KP)).then_inc(w1_in, 16)
            sp.dma_start(w1_raw[KP:KP + 1, 0:N1], b1.rearrange("(a n) -> a n", a=1)).then_inc(w1_in, 16)
            sp.dma_start(w2_raw.rearrange("p (c n) -> p c n", n=N2),
                         w2.rearrange("(c k) n -> k c n", k=P)).then_inc(w2_in, 16)
            load_ids(HOT)
            load_ids(HOT + 1)
            sp.dma_start(wb[:], w_bottom).then_inc(wb_in, 16)
            sp.wait_ge(b2_clear, 1)
            for row in (0, Q):
                sp.dma_start(b2_raw[row:row + 1, :], b2.rearrange("(a n) -> a n", a=1)).then_inc(b2_in, 16)
            sp.dma_start(w3s[:], w3.rearrange("n a -> a n").to_broadcast((P, N2))).then_inc(w3_in, 16)
            for u in range(HOT + 2, UNITS):
                load_ids(u)
            for s in range(T):
                t = TILE_OF[s]
                sp.wait_ge(y_ok, s + 1)
                sp.dma_start(out[t * P:(t + 1) * P, :], y[:, t:t + 1]).then_inc(y_out, 16)
            sp.wait_ge(y_out, 16 * T)

        @block.gpsimd
        def _(pool):
            nc.gpsimd.iota(row_id[:, 0:SUB - 1], [[1, SUB - 1]], base=0, channel_multiplier=SUB - 1,
                           allow_small_or_imprecise_dtypes=True).then_inc(ids_ok, 1)
            nc.gpsimd.iota(row_id[:, SUB - 1:SUB], [[1, 1]], base=FULL, channel_multiplier=1,
                           allow_small_or_imprecise_dtypes=True).then_inc(ids_ok, 1)
            nc.gpsimd.memset(ident[:], 0.0).then_inc(ident_zero, 1)
            pool.wait_ge(ident_zero, 1)
            nc.gpsimd.affine_select(out=ident[:], in_=ident[:], compare_op=ALU.not_equal, fill=1.0, base=0,
                                    pattern=[[-1, P]], channel_multiplier=1).then_inc(ident_ok, 1)
            pool.wait_ge(ids_in, 16)
            for s in range(T):
                for g, group in enumerate(GROUPS):
                    if s >= 2:
                        pool.wait_ge(filled, NTH["turn", s - 2, g] + 1)
                    for f in group:
                        if f:
                            table = FEATS[f] - 1
                            nc.gpsimd.indirect_dma_start(
                                rows[:, s % 2, f - 1, :], None, tables[table],
                                bass.IndirectOffsetOnAxis(idx[:, TILE_OF[s], table:table + 1], 0)
                            ).then_inc(rows_in[s][g], 16)

        @block.tensor
        def _(pe):
            pe.wait_ge(ident_ok, 1)
            for step in ORDER:
                name, s = step[0], step[1]
                if name in ("hot", "turn"):
                    n = NTH[step]
                    if n >= FILL:
                        pe.wait_ge(emptied, n - FILL + 1)
                if name == "hot":
                    u = s
                    h, k = divmod(u, HOT)
                    pe.wait_ge(act_cols, u + 1)
                    pe.wait_ge(dve_cols, u + 1)
                    for part, part_ok in ((hot_hi, hi_ok), (hot_lo, lo_ok)):
                        if h == 0:
                            pe.wait_ge(part_ok, k + 1)
                        for b in range(SUB):
                            kr = P if b < SUB - 1 else REST
                            last = nc.tensor.matmul(psF[n % FILL][:, 0:HB], part[0:kr, k, b, :],
                                                    onehot[0:kr, u % 2, b, :],
                                                    start=(b == 0 and part is hot_hi),
                                                    stop=(b == SUB - 1 and part is hot_lo))
                    last.then_inc(filled, 1)
                elif name == "turn":
                    g = step[2]
                    if g == 0:
                        pe.wait_ge(bottom_in, 16)
                    pe.wait_ge(rows_in[s][g], 16 * len([f for f in GROUPS[g] if f]))
                    for i, f in enumerate(GROUPS[g]):
                        src = rows[:, s % 2, f - 1, :] if f else bot[:, TILE_OF[s], :]
                        last = nc.tensor.transpose(psF[n % FILL][:, i * P:(i + 1) * P], src, ident[:])
                    last.then_inc(filled, 1)
                elif name == "products":
                    pe.wait_ge(emptied, max(NTH["turn", s, NG - 1], NTH["hot", HOT * (1 + s // 2) - 1]) + 1)
                    pe.wait_ge(set_ok, 1)
                    if s >= 1:
                        pe.wait_ge(gram_out, s)
                    slot = SLOT_OF[s]
                    for q in range(Q):
                        for j in range(BLK):
                            at = (Q * j + q) * F
                            last = nc.tensor.matmul(
                                psG[Q * j:Q * j + Q, q // QB, (q % QB) * Q:(q % QB) * Q + Q],
                                emb[:, slot, at:at + Q], emb[:, slot, at:at + Q], start=True, stop=True)
                    last.then_inc(gram_ok, 1)
                elif name == "pairs":
                    pe.wait_ge(pairs_ok, s + 1)
                    if s >= 1:
                        pe.wait_ge(h1_lo_ok, s)
                    for m in range(CH):
                        last = nc.tensor.transpose(psA[0:KP, m * P:(m + 1) * P],
                                                   pairs[:, m * KP:(m + 1) * KP], ident[:])
                    last.then_inc(z_ps, 1)
                elif name == "layer1":
                    if s == 0:
                        pe.wait_ge(w1_hi_ok, 1)
                        pe.wait_ge(w1_lo_ok, 1)
                        pe.wait_ge(wb_in, 16)
                    else:
                        pe.wait_ge(y_ok, s)
                    x = emb[:, SLOT_OF[s], 0:P * F].rearrange("p (b f) -> p f b", f=F)[:, 0, :]
                    nc.tensor.matmul(psB[:], x, wb[:], start=True, stop=False)
                    pe.wait_ge(z_hi_ok, s + 1)
                    for m in range(CH):
                        kr = KP + (m == 0)
                        nc.tensor.matmul(psB[:], z_hi[0:kr, m, :], w1_hi[0:kr, m, :], start=False, stop=False)
                        nc.tensor.matmul(psB[:], z_hi[0:kr, m, :], w1_lo[0:kr, m, :], start=False, stop=False)
                    pe.wait_ge(z_lo_ok, s + 1)
                    for m in range(CH):
                        last = nc.tensor.matmul(psB[:], z_lo[0:KP, m, :], w1_hi[0:KP, m, :],
                                                start=False, stop=(m == CH - 1))
                    last.then_inc(h1_ps, 1)
                elif name == "hidden":
                    pe.wait_ge(h1_ok, s + 1)
                    for c in range(K2):
                        last = nc.tensor.transpose(psA[:, c * P:(c + 1) * P], h1[:, c * P:(c + 1) * P], ident[:])
                    last.then_inc(h1t_ps, 1)
                elif name == "layer2":
                    if s == 0:
                        pe.wait_ge(w2_hi_ok, 1)
                        pe.wait_ge(w2_lo_ok, 1)
                        pe.wait_ge(b2_ok, 1)
                    nc.tensor.matmul(psB[:, 0:N2], ones[:], b2_split[:], start=True, stop=False)
                    pe.wait_ge(h1_hi_ok, s + 1)
                    for c in range(K2):
                        nc.tensor.matmul(psB[:, 0:N2], h1_hi[:, c, :], w2_hi[:, c, :], start=False, stop=False)
                        nc.tensor.matmul(psB[:, 0:N2], h1_hi[:, c, :], w2_lo[:, c, :], start=False, stop=False)
                    pe.wait_ge(h1_lo_ok, s + 1)
                    for c in range(K2):
                        last = nc.tensor.matmul(psB[:, 0:N2], h1_lo[:, c, :], w2_hi[:, c, :],
                                                start=False, stop=(c == K2 - 1))
                    last.then_inc(h2_ps, 1)

        @block.scalar
        def _(act):
            def table_hi(k):
                act.wait_ge(raw_in[k], 32)
                nc.scalar.activation(hot_hi[:, k], raw[:, k % RAW], ACT.Copy).then_inc(hi_ok, 1)

            def columns(u):
                act.wait_ge(spread_in[u % IDS], 16 * (u // IDS + 1))
                if u >= 1:
                    act.wait_ge(act_cols, u)
                for b in range(ACT_SUB):
                    last = nc.scalar.activation(apart[:, b, :], spread[:, u % IDS, :], ACT.Abs,
                                                bias=row_neg[:, b:b + 1])
                last.then_inc(apart_ok, 1)
                act.wait_ge(apart_ok, u + 1)
                if u >= 2:
                    act.wait_ge(filled, NTH["hot", u - 2] + 1)
                nc.scalar.activation(onehot[:, u % 2, 0:ACT_SUB, :], apart[:], ACT.Relu,
                                     bias=1.0, scale=-1.0).then_inc(act_cols, 1)

            act.wait_ge(scrap_ok, 1)
            nc.scalar.activation(scrap[:, 1:2], scrap[:, 0:1], ACT.Abs)
            for u in range(1, IDS):
                act.dma_start(spread[:, u % IDS, :],
                              ids_hot[u:u + 1, 0:HB].to_broadcast((P, HB))).then_inc(spread_in[u % IDS], 16)
            act.wait_ge(neg_ok, 1)
            columns(0)
            table_hi(0)
            table_hi(1)
            for step in ORDER:
                name, s = step[0], step[1]
                if name in ("hot", "turn"):
                    if name == "hot" and s + 1 < UNITS:
                        columns(s + 1)
                        if s + 2 < HOT:
                            table_hi(s + 2)
                    n = NTH[step]
                    act.wait_ge(filled, n + 1)
                if name == "hot":
                    h, k = divmod(s, HOT)
                    if h == 1:
                        act.wait_ge(gram_ok, 1)
                        act.wait_ge(w1_lo_ok, 1)
                        act.wait_ge(w2_lo_ok, 1)
                    dst = emb[:, h:h + 2, 0:P * F].rearrange("p t (b f) -> p f t b", f=F)[:, COLD + k]
                    src = psF[n % FILL][:, 0:HB].rearrange("p (t b) -> p t b", b=P)
                    nc.scalar.activation(dst, src, ACT.Copy).then_inc(emptied, 1)
                    if s == HOT - 1:
                        act.wait_ge(w1_in, 32)
                        nc.scalar.activation(w1_hi[0:KP + 1, 0, :], w1_raw[0:KP + 1, 0:N1], ACT.Copy)
                        nc.scalar.activation(w1_hi[0:KP, 1:CH, :].rearrange("p c n -> p (c n)"),
                                             w1_raw[0:KP, N1:CH * N1], ACT.Copy).then_inc(w1_hi_ok, 1)
                        act.wait_ge(w2_in, 16)
                        nc.scalar.activation(w2_hi[:].rearrange("p c n -> p (c n)"), w2_raw,
                                             ACT.Copy).then_inc(w2_hi_ok, 1)
                        act.wait_ge(b2_in, 32)
                        nc.scalar.activation(b2_split[:], b2_raw[:], ACT.Copy).then_inc(b2_hi_ok, 1)
                elif name == "turn":
                    group = GROUPS[step[2]]
                    if s == 2:
                        act.wait_ge(gram_ok, 1)
                    dst = emb[:, SLOT_OF[s], 0:P * F].rearrange("p (b f) -> p f b", f=F)
                    src = psF[n % FILL][:, 0:len(group) * P].rearrange("p (f b) -> p f b", b=P)
                    nc.scalar.activation(dst[:, group[0]:group[-1] + 1, :], src, ACT.Copy).then_inc(emptied, 1)
                elif name == "pairs":
                    act.wait_ge(z_ps, s + 1)
                    if s >= 1:
                        act.wait_ge(h1_ps, s)
                    nc.scalar.activation(z_hi[0:KP].rearrange("p c b -> p (c b)"), psA[0:KP, 0:CH * P],
                                         ACT.Copy).then_inc(z_hi_ok, 1)
                elif name == "layer1":
                    act.wait_ge(h1_ps, s + 1)
                    if s >= 1:
                        act.wait_ge(h1t_ps, s)
                    nc.scalar.activation(h1[:], psB[:], ACT.Relu).then_inc(h1_ok, 1)
                elif name == "hidden":
                    act.wait_ge(h1t_ps, s + 1)
                    if s >= 1:
                        act.wait_ge(h2_ps, s)
                    nc.scalar.activation(h1_hi[:].rearrange("p c b -> p (c b)"), psA[:],
                                         ACT.Copy).then_inc(h1_hi_ok, 1)

        @block.vector
        def _(dve):
            def table_lo(k):
                dve.wait_ge(hi_ok, k + 1)
                nc.vector.tensor_tensor(hot_lo[:, k], raw[:, k % RAW], hot_hi[:, k].bitcast(F32),
                                        ALU.subtract).then_inc(lo_ok, 1)

            def columns(u):
                dve.wait_ge(spread_in[u % IDS], 16 * (u // IDS + 1))
                if u >= 2:
                    dve.wait_ge(filled, NTH["hot", u - 2] + 1)
                own = SUB - ACT_SUB
                src = spread[:, u % IDS, :]
                row = row_id[:, ACT_SUB:SUB]
                nc.vector.tensor_tensor(onehot[:, u % 2, ACT_SUB:SUB, :],
                                        bass.AP(src.tensor, src.offset, [list(src.ap[0]), [0, own], [1, HB]]),
                                        bass.AP(row.tensor, row.offset, [list(row.ap[0]), [1, own], [0, HB]]),
                                        ALU.is_equal).then_inc(dve_cols, 1)

            nc.vector.memset(scrap[:, 0:1], 0.0).then_inc(scrap_ok, 1)
            nc.vector.memset(raw[P - Q:P, :, SUB - 1, :], 0.0).then_inc(raw_clear, 1)
            dve.wait_ge(ids_ok, 2)
            nc.vector.tensor_scalar(row_neg[:], row_id[:], -1.0, None, ALU.mult).then_inc(neg_ok, 1)
            columns(0)
            nc.vector.memset(ones[:].bitcast(F32), 1.0)
            nc.vector.memset(b2_raw[:], 0.0).then_inc(b2_clear, 1)
            nc.vector.memset(z_hi[:].bitcast(F32), 1.0)
            nc.vector.memset(z_lo[:].bitcast(F32), 0.0)
            nc.vector.memset(emb[:, :, P * F:SPAN], 0.0).then_inc(set_ok, 1)
            table_lo(0)
            for step in ORDER:
                name, s = step[0], step[1]
                if name == "hot" and s + 1 < UNITS:
                    columns(s + 1)
                    if s + 1 < HOT:
                        table_lo(s + 1)
                    if s == HOT - 1:
                        dve.wait_ge(w1_hi_ok, 1)
                        nc.vector.tensor_tensor(w1_lo[0:KP + 1, 0, :], w1_raw[0:KP + 1, 0:N1],
                                                w1_hi[0:KP + 1, 0, :].bitcast(F32), ALU.subtract)
                        nc.vector.tensor_tensor(w1_lo[0:KP, 1:CH, :].rearrange("p c n -> p (c n)"),
                                                w1_raw[0:KP, N1:CH * N1],
                                                w1_hi[0:KP, 1:CH, :].rearrange("p c n -> p (c n)").bitcast(F32),
                                                ALU.subtract).then_inc(w1_lo_ok, 1)
                        dve.wait_ge(w2_hi_ok, 1)
                        nc.vector.tensor_tensor(w2_lo[:].rearrange("p c n -> p (c n)"), w2_raw,
                                                w2_hi[:].rearrange("p c n -> p (c n)").bitcast(F32),
                                                ALU.subtract).then_inc(w2_lo_ok, 1)
                        dve.wait_ge(b2_hi_ok, 1)
                        nc.vector.tensor_tensor(b2_split[Q:Q + 1, :], b2_raw[Q:Q + 1, :],
                                                b2_split[Q:Q + 1, :].bitcast(F32), ALU.subtract).then_inc(b2_ok, 1)
                elif name == "products":
                    dve.wait_ge(gram_ok, s + 1)
                    src = psG[:].rearrange("p c (q f) -> p f c q", f=Q)[:, 0:F]
                    nc.vector.transpose(gram[:, 0:F, :], src).then_inc(gram_out, 1)
                    dve.wait_ge(gram_out, s + 1)
                    nc.vector.tensor_copy(gram[:, F:F + HALF, HALF + 1:F],
                                          gram[:, 0:HALF, HALF + 1:F]).then_inc(wrap_ok, 1)
                    dve.wait_ge(wrap_ok, s + 1)
                    if s >= 1:
                        dve.wait_ge(z_ps, s)
                    g = gram[:]
                    cyclic = bass.AP(g.tensor, g.offset + Q, [list(g.ap[0]), [Q, HALF], [Q + 1, F]])
                    nc.vector.tensor_copy(pairs[:].rearrange("p (s f) -> p s f", f=F), cyclic).then_inc(pairs_ok, 1)
                elif name == "pairs":
                    dve.wait_ge(z_hi_ok, s + 1)
                    if s >= 1:
                        dve.wait_ge(h1_ps, s)
                    nc.vector.tensor_tensor(z_lo[0:KP].rearrange("p c b -> p (c b)"), psA[0:KP, 0:CH * P],
                                            z_hi[0:KP].rearrange("p c b -> p (c b)").bitcast(F32),
                                            ALU.subtract).then_inc(z_lo_ok, 1)
                elif name == "hidden":
                    dve.wait_ge(h1_hi_ok, s + 1)
                    if s >= 1:
                        dve.wait_ge(h2_ps, s)
                    nc.vector.tensor_tensor(h1_lo[:].rearrange("p c b -> p (c b)"), psA[:],
                                            h1_hi[:].rearrange("p c b -> p (c b)").bitcast(F32),
                                            ALU.subtract).then_inc(h1_lo_ok, 1)
                elif name == "layer2":
                    dve.wait_ge(h2_ps, s + 1)
                    if s == 0:
                        dve.wait_ge(w3_in, 16)
                    t = TILE_OF[s]
                    nc.vector.scalar_tensor_tensor(weighed[:], psB[:, 0:N2], 0.0, w3s[:], ALU.max, ALU.mult,
                                                   accum_out=y[:, t:t + 1]).then_inc(y_ok, 1)


def kernel(**inputs):
    import numpy as np
    import concourse.bacc as bacc
    from concourse.bass_utils import run_bass_kernel_spmd

    nc = bacc.Bacc("TRN2", target_bir_lowering=False, num_devices=1)
    arrays = {}

    def dram(name, array):
        arrays[name] = np.ascontiguousarray(array)
        return nc.dram_tensor(name, arrays[name].shape, mybir.dt.from_np(arrays[name].dtype),
                              kind="ExternalInput").ap()

    order, cold = features([inputs[f"tbl_{i}"].shape[0] for i in range(TABLES)])
    w1 = np.asarray(inputs["W_top1"])
    ids = np.asarray(inputs["ids"])
    args = [
        dram("bottom", inputs["r_bottom_output"]),
        dram("ids", ids),
        dram("ids_hot", ids[:, [f - 1 for f in order[cold:]]].T),
        [dram(f"tbl_{i}", inputs[f"tbl_{i}"]) for i in range(TABLES)],
        dram("w_pairs", w1[pair_order(order)]),
        dram("w_bottom", w1[PAIRS:]),
        dram("b_top1", inputs["b_top1"]),
        dram("w_top2", inputs["W_top2"]),
        dram("b_top2", inputs["b_top2"]),
        dram("w_top3", inputs["W_top3"]),
    ]
    out = nc.dram_tensor("scores", (ids.shape[0], 1), F32, kind="ExternalOutput").ap()
    dlrm(nc, *args, out)
    r = run_bass_kernel_spmd(nc, [arrays], core_ids=[0])
    return r.results[0]["scores"]
```
